# Optimizing a Trainium2 kernel written in Bass

```python
import numpy as np
import jax
import jax.numpy as jnp

def _softmax(x, axis=-1):
    return jax.nn.softmax(x, axis=axis)

def _gelu(x):
    return jax.nn.gelu(x, approximate=True)

def _silu(x):
    return jax.nn.silu(x)

def _sigmoid(x):
    return jax.nn.sigmoid(x)

def _layernorm(x, axis=-1, eps=1e-05):
    m = jnp.mean(x, axis=axis, keepdims=True)
    v = jnp.var(x, axis=axis, keepdims=True)
    return (x - m) / jnp.sqrt(v + eps)

def _scatter_add(tgt, idx, src, axis=0):
    return tgt.at[idx].add(src)

def _segment_sum(src, seg, n):
    return jax.ops.segment_sum(src, seg, n)
kernel_name = 'mk_cond_resid_d2_seqx_r4_7130ee'

def setup_inputs(seed: int=0):
    np.random.seed(seed)
    _w = jnp.asarray

    def _rec_inputs():
        import jax
        import jax.numpy as jnp
        _rk = jax.random.key(seed)
        x = -0.0003929 + 0.9999 * jax.random.normal(jax.random.fold_in(_rk, 1), (2, 1024, 256), jnp.float32)
        _lenS = 1024 - jax.random.randint(jax.random.fold_in(_rk, 7), (2,), 0, max(1, 1024 // 4) + 1, jnp.int32)
        _lenS2 = 1024 - jax.random.randint(jax.random.fold_in(_rk, 8), (2,), 0, max(1, 1024 // 4) + 1, jnp.int32)
        itok_B_0_63 = jax.random.randint(jax.random.fold_in(_rk, 11), (2,), 0, 64, jnp.int32)
        itok_B_0_2 = jax.random.randint(jax.random.fold_in(_rk, 12), (2,), 0, 3, jnp.int32)
        return (x, itok_B_0_63, itok_B_0_2)
    x, itok_B_0_63, itok_B_0_2 = _rec_inputs()

    def _L0_cond_setup():
        import jax, jax.numpy as jnp
        import numpy as np
        NUM_CATEGORIES = 64
        INPUT_DIM = 256
        HIDDEN_DIM = 256
        B = 64
        S = 64
        key = jax.random.key(seed)
        kx, kc, kw = jax.random.split(key, 3)
        x = jax.random.normal(kx, (B, S, INPUT_DIM), dtype=jnp.float32)
        cat_ids = jax.random.randint(kc, (B,), 0, NUM_CATEGORIES, dtype=jnp.int32)
        W = 0.02 * jax.random.normal(kw, (NUM_CATEGORIES, INPUT_DIM, HIDDEN_DIM), dtype=jnp.float32)
        b = jnp.zeros((NUM_CATEGORIES, HIDDEN_DIM), dtype=jnp.float32)
        return {'x': x, 'cat_ids': cat_ids, 'W': W, 'b': b}
    _L0_cond_all = _L0_cond_setup()
    _L0_cond_in = {k: v for k, v in _L0_cond_all.items() if k in ('W', 'b')}
    del _L0_cond_all

    def _L1_cond_setup():
        import jax, jax.numpy as jnp
        import numpy as np
        B, S, D, F, E = (8, 512, 256, 1024, 5)

        def _dense(x, wi_, wo_):
            return jax.nn.relu(x @ wi_) @ wo_
        key = jax.random.key(seed)
        ks = jax.random.split(key, 9)
        sc = 0.02
        return {'hidden_states': jax.random.normal(ks[0], (B, S, D), jnp.float32), 'type_label': jax.random.randint(ks[1], (B,), 0, E, jnp.int32), 'wi': jax.random.normal(ks[2], (E, D, F), jnp.float32) * sc, 'wo': jax.random.normal(ks[3], (E, F, D), jnp.float32) * sc, 'swi': jax.random.normal(ks[4], (2, D, F), jnp.float32) * sc, 'swo': jax.random.normal(ks[5], (2, F, D), jnp.float32) * sc, 'g1': jax.random.normal(ks[6], (3 * D, D), jnp.float32) * sc, 'g2': jax.random.normal(ks[7], (D, 3), jnp.float32) * sc}
    _L1_cond_all = _L1_cond_setup()
    _L1_cond_in = {k: v for k, v in _L1_cond_all.items() if k in ('wi', 'wo', 'swi', 'swo', 'g1', 'g2')}
    del _L1_cond_all
    return {'x': x, 'itok_B_0_63': itok_B_0_63, 'itok_B_0_2': itok_B_0_2, 'L0_cond_W': _L0_cond_in['W'], 'L0_cond_b': _L0_cond_in['b'], 'L1_cond_wi': _L1_cond_in['wi'], 'L1_cond_wo': _L1_cond_in['wo'], 'L1_cond_swi': _L1_cond_in['swi'], 'L1_cond_swo': _L1_cond_in['swo'], 'L1_cond_g1': _L1_cond_in['g1'], 'L1_cond_g2': _L1_cond_in['g2']}

def reference(x, itok_B_0_63, itok_B_0_2, L0_cond_W, L0_cond_b, L1_cond_wi, L1_cond_wo, L1_cond_swi, L1_cond_swo, L1_cond_g1, L1_cond_g2):
    import jax
    import jax.numpy as jnp

    def _L0_cond_ref(x, cat_ids, W, b):
        import jax, jax.numpy as jnp
        import numpy as np
        NUM_CATEGORIES = 64
        INPUT_DIM = 256
        HIDDEN_DIM = 256
        B = 64
        S = 64
        selected_W = W[cat_ids]
        selected_b = b[cat_ids]
        out = jnp.einsum('bsd,bdh->bsh', x, selected_W) + selected_b[:, None, :]
        return out

    def _L1_cond_ref(hidden_states, type_label, wi, wo, swi, swo, g1, g2):
        import jax, jax.numpy as jnp
        import numpy as np
        B, S, D, F, E = (8, 512, 256, 1024, 5)

        def _dense(x, wi_, wo_):
            return jax.nn.relu(x @ wi_) @ wo_
        x = hidden_states
        s0 = _dense(x, swi[0], swo[0])
        s1 = _dense(x, swi[1], swo[1])
        wi_sel = wi[type_label]
        wo_sel = wo[type_label]
        h = jax.nn.relu(jnp.einsum('bsd,bdf->bsf', x, wi_sel))
        eo = jnp.einsum('bsf,bfd->bsd', h, wo_sel)
        gate_in = jnp.concatenate([eo[:, 0], s0[:, 0], s1[:, 0]], axis=-1)
        w = jax.nn.softmax(jax.nn.relu(gate_in @ g1) @ g2, axis=-1)
        w = w[:, :, None, None]
        return eo * w[:, 0] + s0 * w[:, 1] + s1 * w[:, 2]
    x = x + _L0_cond_ref(x, itok_B_0_63, L0_cond_W, L0_cond_b)
    x = x + _L1_cond_ref(x, itok_B_0_2, L1_cond_wi, L1_cond_wo, L1_cond_swi, L1_cond_swo, L1_cond_g1, L1_cond_g2)
    return x

_drawn_inputs = setup_inputs


def setup_inputs(seed=0):
    import zlib

    import numpy as np

    out = dict(_drawn_inputs(seed))
    spreads = {'L0_cond_b': (0.0, 0.1)}
    factors = {'L1_cond_g1': 67.871, 'L1_cond_g2': 8.0, 'L1_cond_swi': 2.811}
    for name, (base, spread) in spreads.items():
        noise = np.random.default_rng([zlib.crc32(name.encode()), seed]).standard_normal(out[name].shape)
        drawn = base * np.exp(spread * noise) if base else spread * noise
        out[name] = jnp.asarray(drawn.astype(out[name].dtype))
    for name, factor in factors.items():
        out[name] = (out[name] * factor).astype(out[name].dtype)
    return out
```

```python
from contextlib import ExitStack

import concourse.bass as bass
from concourse import mybir

P = 128
F32 = mybir.dt.float32
F32R = mybir.dt.float32r
I32 = mybir.dt.int32
ALU = mybir.AluOpType
ACT = mybir.ActivationFunctionType
AX = mybir.AxisListType

SHARED = 2
MLPS = SHARED + 1
PIECE_CHUNKS = 2
FIRST_PIECES = 4
LOOKAHEAD = 2


def build(nc, x_t, cat_w, cat_b, mlp_w, mlp_order, cat_ids, g1, g2, out_t):
    B, _, DC, S = x_t.shape
    D = DC * P
    CATS = cat_w.shape[0]
    BANKS, PIECES, _, PIECE = mlp_w.shape
    TOK = 512
    TILES = S // TOK
    FC = PIECES // 2 * PIECE_CHUNKS
    CHUNKS = TILES * MLPS * FC
    TILE_CHUNKS = MLPS * FC
    HRING = LOOKAHEAD + 1
    assert TILES == 2 and CHUNKS % HRING == 0 and PIECE == PIECE_CHUNKS * D == DC * PIECE_CHUNKS * P
    assert B == 2

    N_OPERANDS = (1 + DC, DC)
    N_X1 = TILES * DC
    N_MLP = TILES * MLPS * DC
    N_Y = MLPS * DC
    N_GATE = MLPS * DC

    with ExitStack() as ctx:
        def sb(name, shape, dt=F32):
            return ctx.enter_context(nc.sbuf_tensor(name, shape, dt))

        def psum(name):
            return ctx.enter_context(nc.psum_tensor(name, [P, TOK], F32))

        def sem(name):
            return ctx.enter_context(nc.semaphore(name))

        x_raw = sb("x_raw", [P, DC, S])
        x_hi = sb("x_hi", [P, DC, S], F32R)
        x_lo = sb("x_lo", [P, DC, S], F32R)
        w_raw = sb("w_raw", [P, DC * D])
        w_hi = sb("w_hi", [P, DC * D], F32R)
        w_lo = sb("w_lo", [P, DC * D], F32R)
        bias = sb("bias", [P, B, DC])
        x1 = sb("x1", [P, B, TILES * DC * TOK])
        x1_hi = sb("x1_hi", [P, TILES, DC, TOK], F32R)
        x1_lo = sb("x1_lo", [P, TILES, DC, TOK], F32R)
        staged = sb("staged", [P, PIECES, PIECE])
        m_hi = sb("m_hi", [P, MLPS, PIECES * PIECE], F32R)
        m_lo = sb("m_lo", [P, MLPS, PIECES * PIECE], F32R)
        h_hi = sb("h_hi", [P, HRING, TOK], F32R)
        h_lo = sb("h_lo", [P, HRING, TOK], F32R)
        y = sb("y", [P, MLPS, DC * TOK])
        g1_sb = sb("g1_sb", [P, MLPS * DC, D])
        g2_sb = sb("g2_sb", [P, DC, MLPS])
        gate_part = sb("gate_part", [P, D])
        gate_h = sb("gate_h", [P, DC])
        logit_part = sb("logit_part", [P, 2, MLPS])
        neg_max = sb("neg_max", [P, 1])
        exps = sb("exps", [P, MLPS])
        exp_sum = sb("exp_sum", [P, 1])
        inv_sum = sb("inv_sum", [P, 1])
        mix = sb("mix", [P, MLPS])
        ones = sb("ones", [P, PIECE])

        acc = [[psum(f"acc{i}{d}") for d in range(DC)] for i in range(2)]
        hidden = [psum(f"hidden{i}") for i in range(HRING)]
        gate_ps = psum("gate_ps")

        x_loaded = [[sem(f"x_loaded{t}{d}") for d in range(DC)] for t in range(TILES)]
        w_loaded = sem("w_loaded")
        bias_loaded = sem("bias_loaded")
        piece_loaded = [sem(f"piece_loaded{i}") for i in range(PIECES)]
        g_loaded = sem("g_loaded")
        w_hi_ready = sem("w_hi_ready")
        x_hi_ready = sem("x_hi_ready")
        layer0_operands = [sem(f"layer0_operands{t}") for t in range(TILES)]
        first_piece_hi_ready = sem("first_piece_hi_ready")
        first_pieces_split = sem("first_pieces_split")
        pool_hi = sem("pool_hi")
        pieces_split = sem("pieces_split")
        layer0_done = sem("layer0_done")
        x1_ready = sem("x1_ready")
        x1_hi_ready = sem("x1_hi_ready")
        x1_split = sem("x1_split")
        hidden_done = sem("hidden_done")
        h_hi_ready = sem("h_hi_ready")
        h_split = sem("h_split")
        mlp_done = sem("mlp_done")
        y_ready = sem("y_ready")
        ones_ready = sem("ones_ready")
        gate_sums = sem("gate_sums")
        gate_hidden_done = sem("gate_hidden_done")
        gate_steps = sem("gate_steps")
        logits_done = sem("logits_done")
        neg_max_ready = sem("neg_max_ready")
        exps_ready = sem("exps_ready")
        inv_ready = sem("inv_ready")
        mix_ready = sem("mix_ready")
        tile0_added = sem("tile0_added")
        added_from_acc0 = sem("added_from_acc0")
        added_from_acc1 = sem("added_from_acc1")
        out_written = sem("out_written")

        def x_part(tensor, t, d):
            return tensor[:, d, t * TOK:(t + 1) * TOK]

        def x1_part(b, t, d):
            at = (t * DC + d) * TOK
            return x1[:, bass.ds(b, 1), at:at + TOK].rearrange("p a n -> p (a n)")

        def wi(half, m, d, fc):
            at = 2 * (fc // PIECE_CHUNKS) * PIECE + (d * PIECE_CHUNKS + fc % PIECE_CHUNKS) * P
            return half[:, m, at:at + P]

        def wo(half, m, fc, d):
            at = (2 * (fc // PIECE_CHUNKS) + 1) * PIECE + fc % PIECE_CHUNKS * D + d * P
            return half[:, m, at:at + P]

        def load_x(eng, b):
            for t in range(TILES):
                for d in range(DC):
                    eng.dma_start(x_part(x_raw, t, d), x_part(x_t[b], t, d)).then_inc(x_loaded[t][d], 16)

        def pieces_wait(eng, n, k):
            if k < FIRST_PIECES and isinstance(n, int) and n == 0:
                eng.wait_ge(first_pieces_split, k + 1)
            else:
                eng.wait_ge(pieces_split, n * PIECES + (k + 1 - FIRST_PIECES))

        block = ctx.enter_context(nc.Block())

        @block.sync
        def _(sp):
            def load_layer0(b):
                cat = sp.value_load(cat_ids[0:1, b:b + 1], min_val=0, max_val=CATS - 1)
                if b:
                    sp.wait_ge(layer0_operands[0], b * N_OPERANDS[0])
                    sp.wait_ge(x1_ready, b * N_X1)
                    load_x(sp, b)
                sp.dma_start(w_raw[:], cat_w[bass.ds(cat, 1)].rearrange("a p d n -> p (a d n)")).then_inc(w_loaded, 16)
                sp.dma_start(bias[:, b, :], cat_b[bass.ds(cat, 1)].rearrange("a p d -> p (a d)")).then_inc(bias_loaded, 16)

            def load_mlp(n):
                mlp = sp.value_load(mlp_order[0:1, n:n + 1], min_val=0, max_val=BANKS - 1)
                src = mlp_w[bass.ds(mlp, 1)].rearrange("a k p n -> p (a k) n")
                for k in range(PIECES):
                    if n:
                        pieces_wait(sp, n - 1, k)
                    sp.dma_start(staged[:, k, :], src[:, k, :]).then_inc(piece_loaded[k], 16)

            load_layer0(0)
            load_mlp(0)
            sp.dma_start(g1_sb[:], g1).then_inc(g_loaded, 16)
            sp.dma_start(g2_sb[:], g2).then_inc(g_loaded, 16)
            for n in range(1, MLPS):
                load_mlp(n)
            for b in range(1, B):
                load_layer0(b)
                load_mlp(SHARED + b)

            with sp.Fori(0, B) as b:
                def out_part(t, d, n):
                    return out_t[bass.ds(b, 1), :, d:d + n, t * TOK:(t + 1) * TOK].rearrange("a p d n -> p (a d) n")

                sp.wait_ge(tile0_added, b * MLPS + MLPS)
                sp.dma_start(out_part(0, 0, DC),
                             x1[:, bass.ds(b, 1), 0:DC * TOK].rearrange("p a (d n) -> p (a d) n", d=DC)).then_inc(out_written, 16)
                for d in range(DC):
                    sp.wait_ge(added_from_acc1, b * 2 * DC + 2 * DC + d + 1)
                    sp.dma_start(out_part(1, d, 1).rearrange("p d n -> p (d n)"), x1_part(b, 1, d)).then_inc(out_written, 16)
            sp.wait_ge(out_written, 16 * B * (1 + DC))

        @block.gpsimd
        def _(pool):
            made = [0]

            def split(hi, lo, raw, done):
                nc.gpsimd.tensor_tensor(hi, raw, ones[:], ALU.mult).then_inc(pool_hi, 1)
                made[0] += 1
                pool.wait_ge(pool_hi, made[0])
                nc.gpsimd.tensor_tensor(lo, raw, hi.bitcast(F32), ALU.subtract).then_inc(done, 1)

            def split_mlp(n):
                for k in range(0 if n else FIRST_PIECES, PIECES):
                    pool.wait_ge(piece_loaded[k], 16 * (n + 1))
                    m = min(n, MLPS - 1)
                    split(m_hi[:, m, k * PIECE:(k + 1) * PIECE], m_lo[:, m, k * PIECE:(k + 1) * PIECE],
                          staged[:, k, :], pieces_split)

            for d in range(DC):
                pool.wait_ge(x_hi_ready, DC + d + 1)
                nc.gpsimd.tensor_tensor(x_part(x_lo, 1, d), x_part(x_raw, 1, d), x_part(x_hi, 1, d).bitcast(F32),
                                        ALU.subtract).then_inc(layer0_operands[1], 1)
            pool.wait_ge(ones_ready, 1)
            for n in range(MLPS):
                split_mlp(n)
            for b in range(1, B):
                pool.wait_ge(layer0_done, b * N_X1)
                pool.wait_ge(w_loaded, 16 * (b + 1))
                split(w_hi[:], w_lo[:], w_raw[:], layer0_operands[0])
                for t in range(TILES):
                    for d in range(DC):
                        pool.wait_ge(x_loaded[t][d], 16 * (b + 1))
                        split(x_part(x_hi, t, d), x_part(x_lo, t, d), x_part(x_raw, t, d),
                              layer0_operands[t])
                pool.wait_ge(mlp_done, b * N_MLP)
                split_mlp(SHARED + b)

        @block.scalar
        def _(act):
            load_x(act, 0)
            act.wait_ge(w_loaded, 16)
            nc.scalar.copy(w_hi[:], w_raw[:]).then_inc(w_hi_ready, 1)
            for t in range(TILES):
                for d in range(DC):
                    act.wait_ge(x_loaded[t][d], 16)
                    nc.scalar.copy(x_part(x_hi, t, d), x_part(x_raw, t, d)).then_inc(x_hi_ready, 1)
            for k in range(FIRST_PIECES):
                act.wait_ge(piece_loaded[k], 16)
                nc.scalar.copy(m_hi[:, 0, k * PIECE:(k + 1) * PIECE], staged[:, k, :]).then_inc(first_piece_hi_ready, 1)

            with act.Fori(0, B) as b:
                for t in range(TILES):
                    for d in range(DC):
                        act.wait_ge(x1_ready, b * N_X1 + t * DC + d + 1)
                        nc.scalar.copy(x1_hi[:, t, d, :], x1_part(b, t, d)).then_inc(x1_hi_ready, 1)
                for c in range(CHUNKS):
                    act.wait_ge(hidden_done, b * CHUNKS + c + 1)
                    nc.scalar.activation(h_hi[:, c % HRING, :], hidden[c % HRING][:], ACT.Relu).then_inc(h_hi_ready, 1)
                    m = (c - LOOKAHEAD - 1) // FC
                    if c == (m + 1) * FC + LOOKAHEAD and 0 <= m < MLPS:
                        for d in range(DC):
                            act.wait_ge(mlp_done, b * N_MLP + m * DC + d + 1)
                            nc.scalar.copy(y[:, m, d * TOK:(d + 1) * TOK], acc[m % 2][d][:]).then_inc(y_ready, 1)
                    if c == TILE_CHUNKS + 8:
                        act.wait_ge(logits_done, b + 1)
                        act.wait_ge(neg_max_ready, b + 1)
                        nc.scalar.activation(exps[:], gate_ps[:, 8:8 + MLPS], ACT.Exp, bias=neg_max[:],
                                             accum_out=exp_sum[:]).then_inc(exps_ready, 1)

        @block.vector
        def _(dve):
            nc.vector.memset(ones[:], 1.0).then_inc(ones_ready, 1)
            dve.sem_inc(added_from_acc0, DC)
            dve.sem_inc(added_from_acc1, DC)
            dve.wait_ge(w_hi_ready, 1)
            nc.vector.tensor_tensor(w_lo[:], w_raw[:], w_hi[:].bitcast(F32), ALU.subtract).then_inc(layer0_operands[0], 1)
            for d in range(DC):
                dve.wait_ge(x_hi_ready, d + 1)
                nc.vector.tensor_tensor(x_part(x_lo, 0, d), x_part(x_raw, 0, d), x_part(x_hi, 0, d).bitcast(F32),
                                        ALU.subtract).then_inc(layer0_operands[0], 1)
            for k in range(FIRST_PIECES):
                part = slice(k * PIECE, (k + 1) * PIECE)
                dve.wait_ge(first_piece_hi_ready, k + 1)
                nc.vector.tensor_tensor(m_lo[:, 0, part], staged[:, k, :], m_hi[:, 0, part].bitcast(F32),
                                        ALU.subtract).then_inc(first_pieces_split, 1)

            place = [1, 2, 0]

            with dve.Fori(0, B) as b:
                def gate_partial(m):
                    for d in range(DC):
                        i = m * DC + d
                        row = g1_sb[:, place[m] * DC + d, :]
                        first_token = y[:, m, d * TOK:d * TOK + 1]
                        dve.wait_ge(y_ready, b * N_Y + i + 1)
                        if i == 0:
                            dve.wait_ge(g_loaded, 32)
                            nc.vector.tensor_scalar(gate_part[:], row, first_token, None, ALU.mult).then_inc(gate_sums, 1)
                        else:
                            dve.wait_ge(gate_sums, b * N_GATE + i)
                            nc.vector.scalar_tensor_tensor(out=gate_part[:], in0=row, scalar=first_token, in1=gate_part[:],
                                                           op0=ALU.mult, op1=ALU.add).then_inc(gate_sums, 1)

                def gate_logits():
                    dve.wait_ge(gate_hidden_done, b + 1)
                    nc.vector.tensor_scalar(gate_h[:], gate_ps[:, 0:DC], 0.0, None, ALU.max).then_inc(gate_steps, 1)
                    dve.wait_ge(gate_steps, b * 3 + 1)
                    nc.vector.tensor_scalar(logit_part[:, 0, :], g2_sb[:, 0, :], gate_h[:, 0:1], None, ALU.mult).then_inc(gate_steps, 1)
                    dve.wait_ge(gate_steps, b * 3 + 2)
                    nc.vector.scalar_tensor_tensor(out=logit_part[:, 1, :], in0=g2_sb[:, 1, :], scalar=gate_h[:, 1:2],
                                                   in1=logit_part[:, 0, :], op0=ALU.mult, op1=ALU.add).then_inc(gate_steps, 1)

                def gate_max():
                    dve.wait_ge(logits_done, b + 1)
                    nc.vector.tensor_reduce(neg_max[:], gate_ps[:, 8:8 + MLPS], AX.X, ALU.max,
                                            negate=True).then_inc(neg_max_ready, 1)

                def gate_softmax():
                    dve.wait_ge(exps_ready, b + 1)
                    nc.vector.reciprocal(inv_sum[:], exp_sum[:]).then_inc(inv_ready, 1)
                    dve.wait_ge(inv_ready, b + 1)
                    nc.vector.tensor_scalar(mix[:], exps[:], inv_sum[:, 0:1], None, ALU.mult).then_inc(mix_ready, 1)
                    dve.wait_ge(mix_ready, b + 1)

                def weight(m):
                    return mix[:, place[m]:place[m] + 1]

                def add_tile0(m):
                    total = x1[:, bass.ds(b, 1), 0:DC * TOK].rearrange("p a n -> p (a n)")
                    if m:
                        dve.wait_ge(tile0_added, b * MLPS + m)
                    nc.vector.scalar_tensor_tensor(out=total, in0=y[:, m, :], scalar=weight(m), in1=total,
                                                   op0=ALU.mult, op1=ALU.add).then_inc(tile0_added, 1)

                def add_tile1(m, d):
                    dve.wait_ge(mlp_done, b * N_MLP + (MLPS + m) * DC + d + 1)
                    if m == 1:
                        dve.wait_ge(added_from_acc1, b * 2 * DC + DC + d + 1)
                    if m == 2:
                        dve.wait_ge(added_from_acc0, b * DC + DC + d + 1)
                    pair = (MLPS + m) % 2
                    nc.vector.scalar_tensor_tensor(out=x1_part(b, 1, d), in0=acc[pair][d][:], scalar=weight(m),
                                                   in1=x1_part(b, 1, d), op0=ALU.mult, op1=ALU.add
                                                   ).then_inc(added_from_acc1 if pair else added_from_acc0, 1)

                side = {LOOKAHEAD + FC + 3: [lambda: gate_partial(0)], LOOKAHEAD + 2 * FC + 3: [lambda: gate_partial(1)],
                        TILE_CHUNKS + 3: [lambda: gate_partial(2)], TILE_CHUNKS + 5: [gate_logits],
                        TILE_CHUNKS + 7: [gate_max], TILE_CHUNKS + 9: [gate_softmax]}
                for m in range(MLPS):
                    side[TILE_CHUNKS + 10 + m] = [lambda m=m: add_tile0(m)]
                for d in range(DC):
                    side[TILE_CHUNKS + 13 + d] = [lambda d=d: add_tile1(0, d)]
                    side[TILE_CHUNKS + 20 + d] = [lambda d=d: add_tile1(1, d)]

                dve.wait_ge(bias_loaded, b * 16 + 16)
                for t in range(TILES):
                    for d in range(DC):
                        dve.wait_ge(layer0_done, b * N_X1 + t * DC + d + 1)
                        nc.vector.scalar_tensor_tensor(out=x1_part(b, t, d), in0=acc[t][d][:],
                                                       scalar=bias[:, bass.ds(b, 1), d:d + 1].rearrange("p a d -> p (a d)"),
                                                       in1=x_part(x_raw, t, d), op0=ALU.add, op1=ALU.add).then_inc(x1_ready, 1)
                    for d in range(DC):
                        dve.wait_ge(x1_hi_ready, b * N_X1 + t * DC + d + 1)
                        nc.vector.tensor_tensor(x1_lo[:, t, d, :], x1_part(b, t, d), x1_hi[:, t, d, :].bitcast(F32),
                                                ALU.subtract).then_inc(x1_split, 1)
                for c in range(CHUNKS):
                    dve.wait_ge(h_hi_ready, b * CHUNKS + c + 1)
                    nc.vector.scalar_tensor_tensor(out=h_lo[:, c % HRING, :], in0=hidden[c % HRING][:], scalar=0.0,
                                                   in1=h_hi[:, c % HRING, :].bitcast(F32), op0=ALU.max, op1=ALU.subtract
                                                   ).then_inc(h_split, 1)
                    for work in side.get(c, []):
                        work()
                for d in range(DC):
                    add_tile1(2, d)

        @block.tensor
        def _(pe):
            with pe.Fori(0, B) as b:
                for t in range(TILES):
                    pe.wait_ge((added_from_acc0, added_from_acc1)[t], b * (DC, 2 * DC)[t] + DC)
                    for d in range(DC):
                        for i in range(DC):
                            if d == 0:
                                pe.wait_ge(layer0_operands[t], b * N_OPERANDS[t] + (1 - t) + i + 1)
                            at = i * D + d * P
                            for n, (w, x) in enumerate(((w_hi, x_hi), (w_hi, x_lo), (w_lo, x_hi))):
                                last = nc.tensor.matmul(acc[t][d][:], w[:, at:at + P], x_part(x, t, i),
                                                        start=(i == 0 and n == 0), stop=(i == DC - 1 and n == 2))
                        last.then_inc(layer0_done, 1)

                def hidden_chunk(c):
                    t, m, fc = c // TILE_CHUNKS, c % TILE_CHUNKS // FC, c % FC
                    if t == 0 and fc % PIECE_CHUNKS == 0:
                        piece_wait(m, 2 * (fc // PIECE_CHUNKS))
                    for i in range(DC):
                        if m == 0 and fc == 0:
                            pe.wait_ge(x1_split, b * N_X1 + t * DC + i + 1)
                        for n, (w, x) in enumerate(((m_hi, x1_hi), (m_hi, x1_lo), (m_lo, x1_hi))):
                            last = nc.tensor.matmul(hidden[c % HRING][:], wi(w, m, i, fc), x[:, t, i, :],
                                                    start=(i == 0 and n == 0), stop=(i == DC - 1 and n == 2))
                    last.then_inc(hidden_done, 1)

                def piece_wait(m, k):
                    pieces_wait(pe, b + m if m == MLPS - 1 else m, k)

                def output_chunk(c):
                    t, m, fc = c // TILE_CHUNKS, c % TILE_CHUNKS // FC, c % FC
                    if t == 0 and fc % PIECE_CHUNKS == 0:
                        piece_wait(m, 2 * (fc // PIECE_CHUNKS) + 1)
                    if fc == 0:
                        n = t * MLPS + m
                        if n < 2:
                            pe.wait_ge(x1_ready, b * N_X1 + (n + 1) * DC)
                        elif n < 2 + MLPS:
                            pe.wait_ge(y_ready, b * N_Y + (n - 1) * DC)
                        else:
                            pe.wait_ge(added_from_acc1, b * 2 * DC + 2 * DC)
                    pe.wait_ge(h_split, b * CHUNKS + c + 1)
                    for d in range(DC):
                        for n, (w, h) in enumerate(((m_hi, h_hi), (m_hi, h_lo), (m_lo, h_hi))):
                            last = nc.tensor.matmul(acc[(t * MLPS + m) % 2][d][:], wo(w, m, fc, d), h[:, c % HRING, :],
                                                    start=(fc == 0 and n == 0), stop=(fc == FC - 1 and n == 2))
                        if fc == FC - 1:
                            last.then_inc(mlp_done, 1)

                for c in range(CHUNKS + LOOKAHEAD):
                    if c < CHUNKS:
                        hidden_chunk(c)
                    if c >= LOOKAHEAD:
                        output_chunk(c - LOOKAHEAD)
                    if c == TILE_CHUNKS + 4:
                        pe.wait_ge(gate_sums, b * N_GATE + N_GATE)
                        pe.wait_ge(ones_ready, 1)
                        for d in range(DC):
                            last = nc.tensor.matmul(gate_ps[:, d:d + 1], gate_part[:, d * P:(d + 1) * P], ones[:, 0:1],
                                                    start=True, stop=True)
                        last.then_inc(gate_hidden_done, 1)
                    if c == TILE_CHUNKS + 6:
                        pe.wait_ge(gate_steps, b * 3 + 3)
                        nc.tensor.matmul(gate_ps[:, 8:8 + MLPS], ones[:, 0:P], logit_part[:, 1, :],
                                         start=True, stop=True).then_inc(logits_done, 1)


def kernel(x, itok_B_0_63, itok_B_0_2, L0_cond_W, L0_cond_b, L1_cond_wi, L1_cond_wo, L1_cond_swi, L1_cond_swo,
           L1_cond_g1, L1_cond_g2):
    import numpy as np
    import concourse.bacc as bacc
    from concourse.bass_utils import run_bass_kernel_spmd

    B, S, D = x.shape
    C = L0_cond_W.shape[0]
    E, _, F = L1_cond_wi.shape
    DC, K = D // P, F // (P * PIECE_CHUNKS)

    def feature_major(a, axis):
        a = np.asarray(a)
        return np.swapaxes(a.reshape(*a.shape[:axis], -1, P, *a.shape[axis + 1:]), axis, axis + 1)

    wi_all = np.concatenate([np.asarray(L1_cond_wi), np.asarray(L1_cond_swi)])
    wo_all = np.concatenate([np.asarray(L1_cond_wo), np.asarray(L1_cond_swo)])
    n = len(wi_all)
    wi_pieces = wi_all.reshape(n, DC, P, K, PIECE_CHUNKS * P).transpose(0, 3, 2, 1, 4).reshape(n, K, P, -1)
    wo_pieces = wo_all.reshape(n, K, PIECE_CHUNKS, P, D).transpose(0, 1, 3, 2, 4).reshape(n, K, P, -1)
    arrays = {
        "x_t": np.asarray(x).reshape(B, S, DC, P).transpose(0, 3, 2, 1),
        "cat_w": feature_major(L0_cond_W, 1),
        "cat_b": feature_major(L0_cond_b, 1),
        "mlp_w": np.stack([wi_pieces, wo_pieces], axis=2).reshape(n, 2 * K, P, -1),
        "mlp_order": np.concatenate([np.arange(E, E + SHARED, dtype=np.int32), np.asarray(itok_B_0_2)])[None],
        "cat_ids": np.asarray(itok_B_0_63)[None],
        "g1": feature_major(L1_cond_g1, 0),
        "g2": feature_major(L1_cond_g2, 0),
    }
    arrays = {name: np.ascontiguousarray(a) for name, a in arrays.items()}

    nc = bacc.Bacc("TRN2", target_bir_lowering=False, num_devices=1)
    aps = [nc.dram_tensor(name, a.shape, mybir.dt.from_np(a.dtype), kind="ExternalInput").ap()
           for name, a in arrays.items()]
    out_t = nc.dram_tensor("out_t", (B, P, DC, S), F32, kind="ExternalOutput").ap()
    build(nc, *aps, out_t)
    result = run_bass_kernel_spmd(nc, [arrays], core_ids=[0])
    got = result.results[0]["out_t"]
    return np.ascontiguousarray(got.transpose(0, 3, 2, 1)).reshape(B, S, D)
```

```python
from contextlib import ExitStack

import concourse.bass as bass
from concourse import mybir

P = 128
F32 = mybir.dt.float32
F32R = mybir.dt.float32r
I32 = mybir.dt.int32
ALU = mybir.AluOpType
ACT = mybir.ActivationFunctionType
AX = mybir.AxisListType

SHARED = 2
MLPS = SHARED + 1
PIECE_CHUNKS = 2
FIRST_HI = 3
FIRST_LO = 1
WARMUP = 10
LOOKAHEAD = 2


def build(nc, x_t, cat_w, cat_b, mlp_w, mlp_order, cat_ids, g1, g2, out_t):
    B, _, DC, S = x_t.shape
    D = DC * P
    CATS = cat_w.shape[0]
    BANKS, PIECES, _, PIECE = mlp_w.shape
    TOK = 512
    TILES = S // TOK
    FC = PIECES // 2 * PIECE_CHUNKS
    CHUNKS = TILES * MLPS * FC
    TILE_CHUNKS = MLPS * FC
    HRING = LOOKAHEAD + 1
    assert TILES == 2 and CHUNKS % HRING == 0 and PIECE == PIECE_CHUNKS * D == DC * PIECE_CHUNKS * P
    assert B == 2

    N_X1 = TILES * DC
    N_MLP = TILES * MLPS * DC
    N_Y = MLPS * DC
    N_GATE = MLPS * DC

    with ExitStack() as ctx:
        def sb(name, shape, dt=F32):
            return ctx.enter_context(nc.sbuf_tensor(name, shape, dt))

        def psum(name):
            return ctx.enter_context(nc.psum_tensor(name, [P, TOK], F32))

        def sem(name):
            return ctx.enter_context(nc.semaphore(name))

        x_raw = sb("x_raw", [P, DC, S])
        x_hi = sb("x_hi", [P, DC, S], F32R)
        x_lo = sb("x_lo", [P, DC, S], F32R)
        w_raw = sb("w_raw", [P, DC * D])
        w_hi = sb("w_hi", [P, DC * D], F32R)
        w_lo = sb("w_lo", [P, DC * D], F32R)
        bias = sb("bias", [P, B, DC])
        x1 = sb("x1", [P, B, TILES * DC * TOK])
        x1_hi = sb("x1_hi", [P, TILES, DC, TOK], F32R)
        x1_lo = sb("x1_lo", [P, TILES, DC, TOK], F32R)
        staged = sb("staged", [P, PIECES, PIECE])
        m_hi = sb("m_hi", [P, MLPS, PIECES * PIECE], F32R)
        m_lo = sb("m_lo", [P, MLPS, PIECES * PIECE], F32R)
        h_hi = sb("h_hi", [P, HRING, TOK], F32R)
        h_lo = sb("h_lo", [P, HRING, TOK], F32R)
        y = sb("y", [P, MLPS, DC * TOK])
        g1_sb = sb("g1_sb", [P, MLPS * DC, D])
        g2_sb = sb("g2_sb", [P, DC, MLPS])
        gate_part = sb("gate_part", [P, D])
        gate_h = sb("gate_h", [P, DC])
        logit_part = sb("logit_part", [P, 2, MLPS])
        neg_max = sb("neg_max", [P, 1])
        exps = sb("exps", [P, MLPS])
        exp_sum = sb("exp_sum", [P, 1])
        inv_sum = sb("inv_sum", [P, 1])
        mix = sb("mix", [P, MLPS])
        ones = sb("ones", [P, PIECE])

        acc = [[psum(f"acc{i}{d}") for d in range(DC)] for i in range(2)]
        hidden = [psum(f"hidden{i}") for i in range(HRING)]
        gate_ps = psum("gate_ps")

        x_loaded = [[sem(f"x_loaded{t}{d}") for d in range(DC)] for t in range(TILES)]
        w_loaded = sem("w_loaded")
        bias_loaded = sem("bias_loaded")
        piece_loaded = [sem(f"piece_loaded{i}") for i in range(PIECES)]
        g_loaded = sem("g_loaded")
        w_hi_ready = sem("w_hi_ready")
        tile0_hi_ready = sem("tile0_hi_ready")
        tile1_hi_ready = sem("tile1_hi_ready")
        w_split = sem("w_split")
        x_split = [sem(f"x_split{t}") for t in range(TILES)]
        first_piece_hi_ready = sem("first_piece_hi_ready")
        first_pieces_split = sem("first_pieces_split")
        pool_hi = sem("pool_hi")
        pieces_split = sem("pieces_split")
        layer0_done = sem("layer0_done")
        x1_ready = sem("x1_ready")
        x1_hi_ready = sem("x1_hi_ready")
        x1_split = sem("x1_split")
        hidden_done = sem("hidden_done")
        h_hi_ready = sem("h_hi_ready")
        h_split = sem("h_split")
        mlp_done = sem("mlp_done")
        y_ready = sem("y_ready")
        ones_ready = sem("ones_ready")
        gate_sums = sem("gate_sums")
        gate_hidden_done = sem("gate_hidden_done")
        gate_steps = sem("gate_steps")
        logits_done = sem("logits_done")
        neg_max_ready = sem("neg_max_ready")
        exps_ready = sem("exps_ready")
        inv_ready = sem("inv_ready")
        mix_ready = sem("mix_ready")
        tile0_added = sem("tile0_added")
        added_from_acc0 = sem("added_from_acc0")
        added_from_acc1 = sem("added_from_acc1")
        out_written = sem("out_written")

        def x_part(tensor, t, d):
            return tensor[:, d, t * TOK:(t + 1) * TOK]

        def x1_part(b, t, d):
            at = (t * DC + d) * TOK
            return x1[:, bass.ds(b, 1), at:at + TOK].rearrange("p a n -> p (a n)")

        def wi(half, m, d, fc):
            at = 2 * (fc // PIECE_CHUNKS) * PIECE + (d * PIECE_CHUNKS + fc % PIECE_CHUNKS) * P
            return half[:, m, at:at + P]

        def wo(half, m, fc, d):
            at = (2 * (fc // PIECE_CHUNKS) + 1) * PIECE + fc % PIECE_CHUNKS * D + d * P
            return half[:, m, at:at + P]

        def load_x(eng, b, t):
            for d in range(DC):
                eng.dma_start(x_part(x_raw, t, d), x_part(x_t[b], t, d)).then_inc(x_loaded[t][d], 16)

        def pieces_wait(eng, n, k):
            if isinstance(n, int) and n * PIECES + k < FIRST_LO:
                eng.wait_ge(first_pieces_split, k + 1)
            else:
                eng.wait_ge(pieces_split, n * PIECES + (k + 1 - FIRST_LO))

        block = ctx.enter_context(nc.Block())

        @block.sync
        def _(sp):
            def load_layer0(b):
                cat = sp.value_load(cat_ids[0:1, b:b + 1], min_val=0, max_val=CATS - 1)
                if b:
                    sp.wait_ge(w_split, b)
                    sp.wait_ge(x1_ready, b * N_X1)
                    load_x(sp, b, 0)
                sp.dma_start(w_raw[:], cat_w[bass.ds(cat, 1)].rearrange("a p d n -> p (a d n)")).then_inc(w_loaded, 16)
                load_x(sp, b, 1)
                sp.dma_start(bias[:, b, :], cat_b[bass.ds(cat, 1)].rearrange("a p d -> p (a d)")).then_inc(bias_loaded, 16)

            def load_mlp(n):
                mlp = sp.value_load(mlp_order[0:1, n:n + 1], min_val=0, max_val=BANKS - 1)
                src = mlp_w[bass.ds(mlp, 1)].rearrange("a k p n -> p (a k) n")
                for k in range(PIECES):
                    if n:
                        pieces_wait(sp, n - 1, k)
                    sp.dma_start(staged[:, k, :], src[:, k, :]).then_inc(piece_loaded[k], 16)

            load_layer0(0)
            load_mlp(0)
            sp.dma_start(g1_sb[:], g1).then_inc(g_loaded, 16)
            sp.dma_start(g2_sb[:], g2).then_inc(g_loaded, 16)
            for n in range(1, MLPS):
                load_mlp(n)
            for b in range(1, B):
                load_layer0(b)
                load_mlp(SHARED + b)

            with sp.Fori(0, B) as b:
                def out_part(t, d, n):
                    return out_t[bass.ds(b, 1), :, d:d + n, t * TOK:(t + 1) * TOK].rearrange("a p d n -> p (a d) n")

                sp.wait_ge(tile0_added, b * MLPS + MLPS)
                sp.dma_start(out_part(0, 0, DC),
                             x1[:, bass.ds(b, 1), 0:DC * TOK].rearrange("p a (d n) -> p (a d) n", d=DC)).then_inc(out_written, 16)
                for d in range(DC):
                    sp.wait_ge(added_from_acc1, b * 2 * DC + 2 * DC + d + 1)
                    sp.dma_start(out_part(1, d, 1).rearrange("p d n -> p (d n)"), x1_part(b, 1, d)).then_inc(out_written, 16)
            sp.wait_ge(out_written, 16 * B * (1 + DC))

        @block.gpsimd
        def _(pool):
            made = [0]

            def split(hi, lo, raw, done, count=1):
                hi, lo, raw = (a.rearrange("p (k n) -> p k n", k=count) for a in (hi, lo, raw))
                one = ones[:].unsqueeze(1).broadcast_to([P, count, PIECE])
                nc.gpsimd.tensor_tensor(hi, raw, one, ALU.mult).then_inc(pool_hi, 1)
                made[0] += 1
                pool.wait_ge(pool_hi, made[0])
                nc.gpsimd.tensor_tensor(lo, raw, hi.bitcast(F32), ALU.subtract).then_inc(done, count)

            def split_mlp(n):
                m = min(n, MLPS - 1)
                k = 0 if n else FIRST_LO
                while k < PIECES:
                    count = 1 if n == 0 and k <= FIRST_HI else 2
                    hi, lo = (half[:, m, k * PIECE:(k + count) * PIECE] for half in (m_hi, m_lo))
                    raw = staged[:, k:k + count, :].rearrange("p k n -> p (k n)")
                    if n == 0 and k < FIRST_HI:
                        pool.wait_ge(first_piece_hi_ready, k + 1)
                        nc.gpsimd.tensor_tensor(lo, raw, hi.bitcast(F32), ALU.subtract).then_inc(pieces_split, 1)
                    else:
                        for i in range(k, k + count):
                            pool.wait_ge(piece_loaded[i], 16 * (n + 1))
                        split(hi, lo, raw, pieces_split, count)
                    k += count

            for d in range(DC):
                pool.wait_ge(tile1_hi_ready, d + 1)
                nc.gpsimd.tensor_tensor(x_part(x_lo, 1, d), x_part(x_raw, 1, d), x_part(x_hi, 1, d).bitcast(F32),
                                        ALU.subtract).then_inc(x_split[1], 1)
            pool.wait_ge(ones_ready, 1)
            for n in range(MLPS):
                split_mlp(n)
            for b in range(1, B):
                pool.wait_ge(layer0_done, b * N_X1)
                pool.wait_ge(w_loaded, 16 * (b + 1))
                split(w_hi[:], w_lo[:], w_raw[:], w_split)
                for t in range(TILES):
                    for d in range(DC):
                        pool.wait_ge(x_loaded[t][d], 16 * (b + 1))
                        split(x_part(x_hi, t, d), x_part(x_lo, t, d), x_part(x_raw, t, d), x_split[t])
                pool.wait_ge(mlp_done, b * N_MLP)
                split_mlp(SHARED + b)

        @block.scalar
        def _(act):
            load_x(act, 0, 0)
            act.wait_ge(w_loaded, 16)
            nc.scalar.copy(w_hi[:], w_raw[:]).then_inc(w_hi_ready, 1)
            for d in range(DC):
                act.wait_ge(x_loaded[1][d], 16)
                nc.scalar.copy(x_part(x_hi, 1, d), x_part(x_raw, 1, d)).then_inc(tile1_hi_ready, 1)
            for k in range(FIRST_HI):
                act.wait_ge(piece_loaded[k], 16)
                nc.scalar.copy(m_hi[:, 0, k * PIECE:(k + 1) * PIECE], staged[:, k, :]).then_inc(first_piece_hi_ready, 1)

            with act.Fori(0, B) as b:
                for t in range(TILES):
                    for d in range(DC):
                        act.wait_ge(x1_ready, b * N_X1 + t * DC + d + 1)
                        nc.scalar.copy(x1_hi[:, t, d, :], x1_part(b, t, d)).then_inc(x1_hi_ready, 1)
                for c in range(CHUNKS):
                    act.wait_ge(hidden_done, b * CHUNKS + c + 1)
                    nc.scalar.activation(h_hi[:, c % HRING, :], hidden[c % HRING][:], ACT.Relu).then_inc(h_hi_ready, 1)
                    m = (c - LOOKAHEAD - 1) // FC
                    if c == (m + 1) * FC + LOOKAHEAD and 0 <= m < MLPS:
                        for d in range(DC):
                            act.wait_ge(mlp_done, b * N_MLP + m * DC + d + 1)
                            nc.scalar.copy(y[:, m, d * TOK:(d + 1) * TOK], acc[m % 2][d][:]).then_inc(y_ready, 1)
                    if c == TILE_CHUNKS + 8:
                        act.wait_ge(logits_done, b + 1)
                        act.wait_ge(neg_max_ready, b + 1)
                        nc.scalar.activation(exps[:], gate_ps[:, 8:8 + MLPS], ACT.Exp, bias=neg_max[:],
                                             accum_out=exp_sum[:]).then_inc(exps_ready, 1)

        @block.vector
        def _(dve):
            nc.vector.memset(ones[:], 1.0).then_inc(ones_ready, 1)
            dve.sem_inc(added_from_acc0, DC)
            dve.sem_inc(added_from_acc1, DC)
            for d in range(DC):
                dve.wait_ge(x_loaded[0][d], 16)
                nc.vector.tensor_copy(x_part(x_hi, 0, d), x_part(x_raw, 0, d)).then_inc(tile0_hi_ready, 1)
                dve.wait_ge(tile0_hi_ready, d + 1)
                nc.vector.tensor_tensor(x_part(x_lo, 0, d), x_part(x_raw, 0, d), x_part(x_hi, 0, d).bitcast(F32),
                                        ALU.subtract).then_inc(x_split[0], 1)
            dve.wait_ge(w_hi_ready, 1)
            nc.vector.tensor_tensor(w_lo[:], w_raw[:], w_hi[:].bitcast(F32), ALU.subtract).then_inc(w_split, 1)
            for k in range(FIRST_LO):
                part = slice(k * PIECE, (k + 1) * PIECE)
                dve.wait_ge(first_piece_hi_ready, k + 1)
                nc.vector.tensor_tensor(m_lo[:, 0, part], staged[:, k, :], m_hi[:, 0, part].bitcast(F32),
                                        ALU.subtract).then_inc(first_pieces_split, 1)

            place = [1, 2, 0]

            with dve.Fori(0, B) as b:
                def gate_partial(m):
                    for d in range(DC):
                        i = m * DC + d
                        row = g1_sb[:, place[m] * DC + d, :]
                        first_token = y[:, m, d * TOK:d * TOK + 1]
                        dve.wait_ge(y_ready, b * N_Y + i + 1)
                        if i == 0:
                            dve.wait_ge(g_loaded, 32)
                            nc.vector.tensor_scalar(gate_part[:], row, first_token, None, ALU.mult).then_inc(gate_sums, 1)
                        else:
                            dve.wait_ge(gate_sums, b * N_GATE + i)
                            nc.vector.scalar_tensor_tensor(out=gate_part[:], in0=row, scalar=first_token, in1=gate_part[:],
                                                           op0=ALU.mult, op1=ALU.add).then_inc(gate_sums, 1)

                def gate_logits():
                    dve.wait_ge(gate_hidden_done, b + 1)
                    nc.vector.tensor_scalar(gate_h[:], gate_ps[:, 0:DC], 0.0, None, ALU.max).then_inc(gate_steps, 1)
                    dve.wait_ge(gate_steps, b * 3 + 1)
                    nc.vector.tensor_scalar(logit_part[:, 0, :], g2_sb[:, 0, :], gate_h[:, 0:1], None, ALU.mult).then_inc(gate_steps, 1)
                    dve.wait_ge(gate_steps, b * 3 + 2)
                    nc.vector.scalar_tensor_tensor(out=logit_part[:, 1, :], in0=g2_sb[:, 1, :], scalar=gate_h[:, 1:2],
                                                   in1=logit_part[:, 0, :], op0=ALU.mult, op1=ALU.add).then_inc(gate_steps, 1)

                def gate_max():
                    dve.wait_ge(logits_done, b + 1)
                    nc.vector.tensor_reduce(neg_max[:], gate_ps[:, 8:8 + MLPS], AX.X, ALU.max,
                                            negate=True).then_inc(neg_max_ready, 1)

                def gate_softmax():
                    dve.wait_ge(exps_ready, b + 1)
                    nc.vector.reciprocal(inv_sum[:], exp_sum[:]).then_inc(inv_ready, 1)
                    dve.wait_ge(inv_ready, b + 1)
                    nc.vector.tensor_scalar(mix[:], exps[:], inv_sum[:, 0:1], None, ALU.mult).then_inc(mix_ready, 1)
                    dve.wait_ge(mix_ready, b + 1)

                def weight(m):
                    return mix[:, place[m]:place[m] + 1]

                def add_tile0(m):
                    total = x1[:, bass.ds(b, 1), 0:DC * TOK].rearrange("p a n -> p (a n)")
                    if m:
                        dve.wait_ge(tile0_added, b * MLPS + m)
                    nc.vector.scalar_tensor_tensor(out=total, in0=y[:, m, :], scalar=weight(m), in1=total,
                                                   op0=ALU.mult, op1=ALU.add).then_inc(tile0_added, 1)

                def add_tile1(m, d):
                    dve.wait_ge(mlp_done, b * N_MLP + (MLPS + m) * DC + d + 1)
                    if m == 1:
                        dve.wait_ge(added_from_acc1, b * 2 * DC + DC + d + 1)
                    if m == 2:
                        dve.wait_ge(added_from_acc0, b * DC + DC + d + 1)
                    pair = (MLPS + m) % 2
                    nc.vector.scalar_tensor_tensor(out=x1_part(b, 1, d), in0=acc[pair][d][:], scalar=weight(m),
                                                   in1=x1_part(b, 1, d), op0=ALU.mult, op1=ALU.add
                                                   ).then_inc(added_from_acc1 if pair else added_from_acc0, 1)

                dve.wait_ge(bias_loaded, b * 16 + 16)
                for t in range(TILES):
                    for d in range(DC):
                        dve.wait_ge(layer0_done, b * N_X1 + t * DC + d + 1)
                        nc.vector.scalar_tensor_tensor(out=x1_part(b, t, d), in0=acc[t][d][:],
                                                       scalar=bias[:, bass.ds(b, 1), d:d + 1].rearrange("p a d -> p (a d)"),
                                                       in1=x_part(x_raw, t, d), op0=ALU.add, op1=ALU.add).then_inc(x1_ready, 1)
                    for d in range(DC):
                        dve.wait_ge(x1_hi_ready, b * N_X1 + t * DC + d + 1)
                        nc.vector.tensor_tensor(x1_lo[:, t, d, :], x1_part(b, t, d), x1_hi[:, t, d, :].bitcast(F32),
                                                ALU.subtract).then_inc(x1_split, 1)
                for c in range(CHUNKS):
                    dve.wait_ge(h_hi_ready, b * CHUNKS + c + 1)
                    nc.vector.scalar_tensor_tensor(out=h_lo[:, c % HRING, :], in0=hidden[c % HRING][:], scalar=0.0,
                                                   in1=h_hi[:, c % HRING, :].bitcast(F32), op0=ALU.max, op1=ALU.subtract
                                                   ).then_inc(h_split, 1)
                    for m in range(MLPS):
                        if c == (m + 1) * FC + LOOKAHEAD + 1:
                            gate_partial(m)
                    if c == TILE_CHUNKS + 5:
                        gate_logits()
                    if c == TILE_CHUNKS + 7:
                        gate_max()
                    if c == TILE_CHUNKS + 9:
                        gate_softmax()
                    if TILE_CHUNKS + 10 <= c < TILE_CHUNKS + 10 + MLPS:
                        add_tile0(c - (TILE_CHUNKS + 10))
                    for m, first in ((0, TILE_CHUNKS + 13), (1, TILE_CHUNKS + 20)):
                        if first <= c < first + DC:
                            add_tile1(m, c - first)
                for d in range(DC):
                    add_tile1(2, d)

        @block.tensor
        def _(pe):
            pe.wait_ge(ones_ready, 1)
            for _ in range(WARMUP):
                nc.tensor.matmul(gate_ps[:, 0:P], ones[:, 0:P], ones[:, 0:P], start=True, stop=True)
            with pe.Fori(0, B) as b:
                for t in range(TILES):
                    pe.wait_ge((added_from_acc0, added_from_acc1)[t], b * (DC, 2 * DC)[t] + DC)
                    for d in range(DC):
                        passes = [(w_hi, x, i) for i in range(DC) for x in (x_hi, x_lo)] + [(w_lo, x_hi, i) for i in range(DC)]
                        for n, (w, x, i) in enumerate(passes):
                            if t == d == n == 0:
                                pe.wait_ge(w_hi_ready, 1)
                            if d == 0 and w is w_hi and x is x_hi:
                                pe.wait_ge(x_split[t], b * DC + i + 1)
                            if d == 0 and n == 2 * DC:
                                pe.wait_ge(w_split, b + 1)
                            at = i * D + d * P
                            last = nc.tensor.matmul(acc[t][d][:], w[:, at:at + P], x_part(x, t, i),
                                                    start=(n == 0), stop=(n == len(passes) - 1))
                        last.then_inc(layer0_done, 1)

                def hidden_chunk(c):
                    t, m, fc = c // TILE_CHUNKS, c % TILE_CHUNKS // FC, c % FC
                    if t == 0 and fc % PIECE_CHUNKS == 0:
                        piece_wait(m, 2 * (fc // PIECE_CHUNKS))
                    for i in range(DC):
                        if m == 0 and fc == 0:
                            pe.wait_ge(x1_split, b * N_X1 + t * DC + i + 1)
                        for n, (w, x) in enumerate(((m_hi, x1_hi), (m_hi, x1_lo), (m_lo, x1_hi))):
                            last = nc.tensor.matmul(hidden[c % HRING][:], wi(w, m, i, fc), x[:, t, i, :],
                                                    start=(i == 0 and n == 0), stop=(i == DC - 1 and n == 2))
                    last.then_inc(hidden_done, 1)

                def piece_wait(m, k):
                    pieces_wait(pe, b + m if m == MLPS - 1 else m, k)

                def output_chunk(c):
                    t, m, fc = c // TILE_CHUNKS, c % TILE_CHUNKS // FC, c % FC
                    if t == 0 and fc % PIECE_CHUNKS == 0:
                        piece_wait(m, 2 * (fc // PIECE_CHUNKS) + 1)
                    if fc == 0:
                        n = t * MLPS + m
                        if n < 2:
                            pe.wait_ge(x1_ready, b * N_X1 + (n + 1) * DC)
                        elif n < 2 + MLPS:
                            pe.wait_ge(y_ready, b * N_Y + (n - 1) * DC)
                        else:
                            pe.wait_ge(added_from_acc1, b * 2 * DC + 2 * DC)
                    pe.wait_ge(h_split, b * CHUNKS + c + 1)
                    for d in range(DC):
                        for n, (w, h) in enumerate(((m_hi, h_hi), (m_hi, h_lo), (m_lo, h_hi))):
                            last = nc.tensor.matmul(acc[(t * MLPS + m) % 2][d][:], wo(w, m, fc, d), h[:, c % HRING, :],
                                                    start=(fc == 0 and n == 0), stop=(fc == FC - 1 and n == 2))
                        if fc == FC - 1:
                            last.then_inc(mlp_done, 1)

                for c in range(CHUNKS + LOOKAHEAD):
                    if c < CHUNKS:
                        hidden_chunk(c)
                    if c >= LOOKAHEAD:
                        output_chunk(c - LOOKAHEAD)
                    if c == TILE_CHUNKS + 4:
                        pe.wait_ge(gate_sums, b * N_GATE + N_GATE)
                        for d in range(DC):
                            last = nc.tensor.matmul(gate_ps[:, d:d + 1], gate_part[:, d * P:(d + 1) * P], ones[:, 0:1],
                                                    start=True, stop=True)
                        last.then_inc(gate_hidden_done, 1)
                    if c == TILE_CHUNKS + 6:
                        pe.wait_ge(gate_steps, b * 3 + 3)
                        nc.tensor.matmul(gate_ps[:, 8:8 + MLPS], ones[:, 0:P], logit_part[:, 1, :],
                                         start=True, stop=True).then_inc(logits_done, 1)


def kernel(x, itok_B_0_63, itok_B_0_2, L0_cond_W, L0_cond_b, L1_cond_wi, L1_cond_wo, L1_cond_swi, L1_cond_swo,
           L1_cond_g1, L1_cond_g2):
    import numpy as np
    import concourse.bacc as bacc
    from concourse.bass_utils import run_bass_kernel_spmd

    B, S, D = x.shape
    C = L0_cond_W.shape[0]
    E, _, F = L1_cond_wi.shape
    DC, K = D // P, F // (P * PIECE_CHUNKS)

    def feature_major(a, axis):
        a = np.asarray(a)
        return np.swapaxes(a.reshape(*a.shape[:axis], -1, P, *a.shape[axis + 1:]), axis, axis + 1)

    wi_all = np.concatenate([np.asarray(L1_cond_wi), np.asarray(L1_cond_swi)])
    wo_all = np.concatenate([np.asarray(L1_cond_wo), np.asarray(L1_cond_swo)])
    n = len(wi_all)
    wi_pieces = wi_all.reshape(n, DC, P, K, PIECE_CHUNKS * P).transpose(0, 3, 2, 1, 4).reshape(n, K, P, -1)
    wo_pieces = wo_all.reshape(n, K, PIECE_CHUNKS, P, D).transpose(0, 1, 3, 2, 4).reshape(n, K, P, -1)
    arrays = {
        "x_t": np.asarray(x).reshape(B, S, DC, P).transpose(0, 3, 2, 1),
        "cat_w": feature_major(L0_cond_W, 1),
        "cat_b": feature_major(L0_cond_b, 1),
        "mlp_w": np.stack([wi_pieces, wo_pieces], axis=2).reshape(n, 2 * K, P, -1),
        "mlp_order": np.concatenate([np.arange(E, E + SHARED, dtype=np.int32), np.asarray(itok_B_0_2)])[None],
        "cat_ids": np.asarray(itok_B_0_63)[None],
        "g1": feature_major(L1_cond_g1, 0),
        "g2": feature_major(L1_cond_g2, 0),
    }
    arrays = {name: np.ascontiguousarray(a) for name, a in arrays.items()}

    nc = bacc.Bacc("TRN2", target_bir_lowering=False, num_devices=1)
    aps = [nc.dram_tensor(name, a.shape, mybir.dt.from_np(a.dtype), kind="ExternalInput").ap()
           for name, a in arrays.items()]
    out_t = nc.dram_tensor("out_t", (B, P, DC, S), F32, kind="ExternalOutput").ap()
    build(nc, *aps, out_t)
    result = run_bass_kernel_spmd(nc, [arrays], core_ids=[0])
    got = result.results[0]["out_t"]
    return np.ascontiguousarray(got.transpose(0, 3, 2, 1)).reshape(B, S, D)
```
